# Optimizing a Trainium2 kernel written in Bass

```python
import numpy as np
import jax
import jax.numpy as jnp

def _softmax(x, axis=-1):
    return jax.nn.softmax(x, axis=axis)

def _gelu(x):
    return jax.nn.gelu(x, approximate=True)

def _silu(x):
    return jax.nn.silu(x)

def _sigmoid(x):
    return jax.nn.sigmoid(x)

def _layernorm(x, axis=-1, eps=1e-05):
    m = jnp.mean(x, axis=axis, keepdims=True)
    v = jnp.var(x, axis=axis, keepdims=True)
    return (x - m) / jnp.sqrt(v + eps)

def _scatter_add(tgt, idx, src, axis=0):
    return tgt.at[idx].add(src)

def _segment_sum(src, seg, n):
    return jax.ops.segment_sum(src, seg, n)
kernel_name = 'mk_adj_resnorm_d2_adj_r2_888a3c'

def setup_inputs(seed: int=0):
    np.random.seed(seed)
    _w = jnp.asarray

    def _rec_inputs():
        import jax
        import jax.numpy as jnp
        _gk = jax.random.key(seed)
        x = -0.0002928 + 1 * jax.random.normal(jax.random.fold_in(_gk, 1), (32, 256, 256), jnp.float32)
        _w = (1.0 + jnp.arange(256, dtype=jnp.float32)) ** (-0.5)
        _w = _w / _w.mean()
        _pij = jnp.clip(0.03125 * _w[:, None] * _w[None, :], 0.0, 1.0)
        _a = jax.random.uniform(jax.random.fold_in(_gk, 2), (32, 256, 256)) < _pij
        adj = _a
        return (x, adj)
    x, adj = _rec_inputs()

    def _L0_gnn_setup():
        import jax, jax.numpy as jnp
        import numpy as np
        QUERY_DIM = 256
        HEADS = 4
        DIM_HEAD = 64
        INNER = HEADS * DIM_HEAD
        B, N = (4, 1024)
        key = jax.random.key(seed)
        ks = jax.random.split(key, 6)
        s = 1.0 / np.sqrt(QUERY_DIM)
        x = jax.random.normal(ks[0], (B, N, QUERY_DIM), dtype=jnp.float32)
        adjacency_mask = jax.random.randint(ks[1], (B, N, N), 0, 2) > 0
        Wq = jax.random.normal(ks[2], (QUERY_DIM, INNER), dtype=jnp.float32) * s
        Wk = jax.random.normal(ks[3], (QUERY_DIM, INNER), dtype=jnp.float32) * s
        Wv = jax.random.normal(ks[4], (QUERY_DIM, INNER), dtype=jnp.float32) * s
        Wo = jax.random.normal(ks[5], (INNER, QUERY_DIM), dtype=jnp.float32) * (1.0 / np.sqrt(INNER))
        bo = jnp.zeros((QUERY_DIM,), dtype=jnp.float32)
        return {'x': x, 'adjacency_mask': adjacency_mask, 'Wq': Wq, 'Wk': Wk, 'Wv': Wv, 'Wo': Wo, 'bo': bo}
    _L0_gnn_all = _L0_gnn_setup()
    _L0_gnn_in = {k: v for k, v in _L0_gnn_all.items() if k in ('Wq', 'Wk', 'Wv', 'Wo', 'bo')}
    del _L0_gnn_all

    def _L1_gnn_setup():
        import jax, jax.numpy as jnp
        import numpy as np
        EMB = 256
        HEADS = 8
        HEAD_DIM = 64
        INNER = HEADS * HEAD_DIM
        B, S = (2, 1024)
        SCALE = HEAD_DIM ** (-0.5)
        MIN_SCORE = -1000000000.0
        LN_EPS = 1e-05
        key = jax.random.key(seed)
        ks = jax.random.split(key, 6)
        x = jax.random.normal(ks[0], (B, S, EMB), dtype=jnp.float32)
        graph_mask = jax.random.uniform(ks[1], (B, S, S)) < 0.05
        gamma = jnp.ones((EMB,), jnp.float32)
        beta = jnp.zeros((EMB,), jnp.float32)
        w_qkv = jax.random.normal(ks[2], (3 * INNER, EMB), jnp.float32) * EMB ** (-0.5)
        w_out = jax.random.normal(ks[3], (EMB, INNER), jnp.float32) * INNER ** (-0.5)
        b_out = jnp.zeros((EMB,), jnp.float32)
        return {'x': x, 'graph_mask': graph_mask, 'gamma': gamma, 'beta': beta, 'w_qkv': w_qkv, 'w_out': w_out, 'b_out': b_out}
    _L1_gnn_all = _L1_gnn_setup()
    _L1_gnn_in = {k: v for k, v in _L1_gnn_all.items() if k in ('gamma', 'beta', 'w_qkv', 'w_out', 'b_out')}
    del _L1_gnn_all
    return {'x': x, 'adj': adj, 'L0_gnn_Wq': _L0_gnn_in['Wq'], 'L0_gnn_Wk': _L0_gnn_in['Wk'], 'L0_gnn_Wv': _L0_gnn_in['Wv'], 'L0_gnn_Wo': _L0_gnn_in['Wo'], 'L0_gnn_bo': _L0_gnn_in['bo'], 'L1_gnn_gamma': _L1_gnn_in['gamma'], 'L1_gnn_beta': _L1_gnn_in['beta'], 'L1_gnn_w_qkv': _L1_gnn_in['w_qkv'], 'L1_gnn_w_out': _L1_gnn_in['w_out'], 'L1_gnn_b_out': _L1_gnn_in['b_out']}

def reference(x, adj, L0_gnn_Wq, L0_gnn_Wk, L0_gnn_Wv, L0_gnn_Wo, L0_gnn_bo, L1_gnn_gamma, L1_gnn_beta, L1_gnn_w_qkv, L1_gnn_w_out, L1_gnn_b_out):
    import jax
    import jax.numpy as jnp

    def _L0_gnn_ref(x, adjacency_mask, Wq, Wk, Wv, Wo, bo):
        import jax, jax.numpy as jnp
        import numpy as np
        QUERY_DIM = 256
        HEADS = 4
        DIM_HEAD = 64
        INNER = HEADS * DIM_HEAD
        B, N = (4, 1024)
        scale = DIM_HEAD ** (-0.5)

        def split_heads(t):
            b, n, _ = t.shape
            return t.reshape(b, n, HEADS, DIM_HEAD).transpose(0, 2, 1, 3)
        q = split_heads(x @ Wq)
        k = split_heads(x @ Wk)
        v = split_heads(x @ Wv)
        sim = jnp.einsum('bhid,bhjd->bhij', q, k) * scale
        neg = -jnp.finfo(sim.dtype).max
        sim = jnp.where(adjacency_mask[:, None, :, :], sim, neg)
        attn = jax.nn.softmax(sim, axis=-1)
        out = jnp.einsum('bhij,bhjd->bhid', attn, v)
        out = out.transpose(0, 2, 1, 3).reshape(x.shape[0], x.shape[1], INNER)
        return out @ Wo + bo

    def _L1_gnn_ref(x, graph_mask, gamma, beta, w_qkv, w_out, b_out):
        import jax, jax.numpy as jnp
        import numpy as np
        EMB = 256
        HEADS = 8
        HEAD_DIM = 64
        INNER = HEADS * HEAD_DIM
        B, S = (2, 1024)
        SCALE = HEAD_DIM ** (-0.5)
        MIN_SCORE = -1000000000.0
        LN_EPS = 1e-05
        bsz, seq_len, _ = x.shape
        mu = jnp.mean(x, axis=-1, keepdims=True)
        var = jnp.mean(jnp.square(x - mu), axis=-1, keepdims=True)
        h = (x - mu) * jax.lax.rsqrt(var + LN_EPS) * gamma + beta
        qkv = h @ w_qkv.T
        q, k, v = jnp.split(qkv, 3, axis=-1)
        q = q.reshape(bsz, seq_len, HEADS, HEAD_DIM)
        k = k.reshape(bsz, seq_len, HEADS, HEAD_DIM)
        v = v.reshape(bsz, seq_len, HEADS, HEAD_DIM)
        scores = jnp.einsum('bihd,bjhd->bhij', q, k) * SCALE
        eye = jnp.eye(seq_len, dtype=bool)[None]
        mask = graph_mask | eye
        scores = jnp.where(mask[:, None], scores, MIN_SCORE)
        probs = jax.nn.softmax(scores, axis=-1)
        out = jnp.einsum('bhij,bjhd->bihd', probs, v)
        out = out.reshape(bsz, seq_len, INNER)
        return out @ w_out.T + b_out
    x = _layernorm(x + _L0_gnn_ref(x, adj, L0_gnn_Wq, L0_gnn_Wk, L0_gnn_Wv, L0_gnn_Wo, L0_gnn_bo), axis=-1)
    x = _layernorm(x + _L1_gnn_ref(x, adj, L1_gnn_gamma, L1_gnn_beta, L1_gnn_w_qkv, L1_gnn_w_out, L1_gnn_b_out), axis=-1)
    return x

_drawn_inputs = setup_inputs


def setup_inputs(seed=0):
    import zlib

    import numpy as np

    out = dict(_drawn_inputs(seed))
    spreads = {'L0_gnn_bo': (0.0, 0.1),
     'L1_gnn_gamma': (1.0, 0.2),
     'L1_gnn_beta': (0.0, 0.1),
     'L1_gnn_b_out': (0.0, 0.1)}
    factors = {}
    for name, (base, spread) in spreads.items():
        noise = np.random.default_rng([zlib.crc32(name.encode()), seed]).standard_normal(out[name].shape)
        drawn = base * np.exp(spread * noise) if base else spread * noise
        out[name] = jnp.asarray(drawn.astype(out[name].dtype))
    for name, factor in factors.items():
        out[name] = (out[name] * factor).astype(out[name].dtype)
    return out
```

```python
from contextlib import ExitStack

import numpy as np

import concourse.bass as bass
from concourse import mybir

GRAPHS, NODES, DIM = 32, 256, 256
P = 128
CH = NODES // P
HEAD = 64
HEADS = (4, 8)
PAIRS = (2, 4)
SLOTS = PAIRS[0] + PAIRS[1]
INNER = (HEADS[0] * HEAD, HEADS[1] * HEAD)
PROJ = (3, 6)
EPS = 1e-5
SCALE = HEAD ** -0.5
MASKED0 = float(np.finfo(np.float32).max)
MASKED1 = 1e9 / SCALE
LARGEST = 3.0e38

BEFORE = (
    (("xt", 0, 0, 1),),
    (("proj", 0, 0, 1),),
    (("proj", 1, 2, -1),),
    (),
    (("wo", 0, 0, 0),),
    (("wo", 1, 0, -2),),
)
AFTER = (
    (("ht", 1, 0, -1),),
    (("proj", 1, 0, -1), ("proj", 1, 1, -1)),
    (("proj", 1, 3, -1),),
    (("proj", 0, 1, 1),),
    (("proj", 1, 4, -1), ("proj", 1, 5, -1)),
    (("proj", 0, 2, 1),),
)
SLOT = ((0, 0, 0), (0, 0, 1), (1, -2, 3), (1, -1, 0), (1, -1, 1), (1, -1, 2))


def slot_of(k):
    layer, d, pair = SLOT[k % SLOTS]
    return layer, d + k // SLOTS, pair


def bank_users():
    users = []
    for k in range(SLOTS):
        layer, d, pair = slot_of(k - 2)
        users += [*BEFORE[k], ("pv", layer, pair, d), *AFTER[k]]
    return users


USERS = bank_users()
BANKS = 4
ORDER_L1 = ("q", 0), ("k", 0), ("q", 1), ("k", 1), ("v", 0), ("v", 1)
ORDER_L0 = ("q", 0), ("k", 0), ("v", 0)


class Step:

    def __init__(self, t=None, r=None, j=None, first=None):
        self.t, self.r, self.j = t, r, j
        self.first = first

    def has(self, d):
        return self.r is not None or 0 <= self.t + d < GRAPHS

    def parity(self, d):
        return ((self.t if self.r is None else self.j) + d) % 2

    def graph(self, d):
        return self.t + d if self.r is None else self.r * 2 + (self.j + d)

    def count(self, per, d, n):
        if self.r is None:
            return per * (self.t + d) + n
        assert 2 * per * self.first + per * (self.j + d) + n > 0
        return self.r * (2 * per) + (per * (self.j + d) + n)

    def head(self, unit, hh):
        layer, d, pair = unit
        return self.count(HEADS[layer], d, 2 * pair + hh + 1)

    def dma(self, d):
        if self.r is None:
            return 16 * ((self.t + d) // 2 + 1)
        return self.r * 16 + 16 * ((self.j + d) // 2 + 1)

    def hold(self, eng, held):
        if self.r is not None:
            eng.sem_inc(held, 1)


def build(nc, x, adj, wq0, wk0, wv0, wo0, bo0, gamma, beta, wqkv1, wo1, bo1, out):
    f32, f32r, u8 = mybir.dt.float32, mybir.dt.float32r, mybir.dt.uint8
    ALU, ACT = mybir.AluOpType, mybir.ActivationFunctionType

    x_v = x.rearrange("b (c p) e -> b p c e", p=P)
    adj_v = adj.rearrange("b (c p) j -> b p c j", p=P)
    out_v = out.rearrange("b (c p) e -> b p c e", p=P)

    ctx = ExitStack()
    with ctx:
        def sb(name, shape, dt=f32):
            return ctx.enter_context(nc.sbuf_tensor(name, shape, dt))

        def sem(name):
            return ctx.enter_context(nc.semaphore(name))

        W_NAMES = ("q0", "k0", "v0", "o0", "qkv1", "o1")
        SPLIT_AT = {"start": W_NAMES[0:3], (-1, 5): ("o0",), (0, 3): ("qkv1",), (0, 4): ("o1",)}
        W_SHAPE = {"q0": (CH, INNER[0]), "k0": (CH, INNER[0]), "v0": (CH, INNER[0]), "o0": (INNER[0] // P, DIM),
                   "qkv1": (CH, 3 * INNER[1]), "o1": (INNER[1] // P, DIM)}
        W_DRAM = {"q0": wq0, "k0": wk0, "v0": wv0, "o0": wo0, "qkv1": wqkv1, "o1": wo1}
        w_raw = {n: sb(f"w_raw_{n}", [P, *W_SHAPE[n]]) for n in W_NAMES}
        w_hi = {n: sb(f"w_hi_{n}", [P, *W_SHAPE[n]], f32r) for n in W_NAMES}
        w_lo = {n: sb(f"w_lo_{n}", [P, *W_SHAPE[n]], f32r) for n in W_NAMES}
        ident = sb("ident", [P, P])
        minus_half = sb("minus_half", [P, CH])
        gamma_sb = sb("gamma_sb", [P, CH])
        beta_sb = sb("beta_sb", [P, CH])
        bias_sb = [sb(f"bias_sb{n}", [P, DIM]) for n in range(2)]

        x_in = [sb(f"x_in{i}", [P, CH, DIM]) for i in range(2)]
        adj_in = [sb(f"adj_in{i}", [P, CH, NODES], u8) for i in range(2)]
        mask = [[sb(f"mask{n}_{i}", [P, CH, NODES]) for i in range(2)] for n in range(2)]
        xt_hi = [sb(f"xt_hi{n}", [P, CH, NODES], f32r) for n in range(2)]
        xt_lo = [sb(f"xt_lo{n}", [P, CH, NODES], f32r) for n in range(2)]
        ht = sb("ht", [P, CH, NODES])
        qk_hi = [{c: sb(f"{c}_hi{n}", [P, PAIRS[n], NODES], f32r) for c in "qk"} for n in range(2)]
        qk_lo = [{c: sb(f"{c}_lo{n}", [P, PAIRS[n], NODES], f32r) for c in "qk"} for n in range(2)]
        v_hi = [sb(f"v_hi{n}", [P, CH, HEADS[n] * P], f32r) for n in range(2)]
        v_lo = [sb(f"v_lo{n}", [P, CH, HEADS[n] * P], f32r) for n in range(2)]
        ot_hi = [sb(f"ot_hi{n}", [P, PAIRS[n], NODES], f32r) for n in range(2)]
        ot_lo = [sb(f"ot_lo{n}", [P, PAIRS[n], NODES], f32r) for n in range(2)]
        probs = [sb(f"probs{i}", [P, 2, CH, NODES]) for i in range(2)]
        negmax = [sb(f"negmax{i}", [P, 2, CH]) for i in range(2)]
        sums = [sb(f"sums{i}", [P, 2, CH]) for i in range(2)]
        rsums = [sb(f"rsums{i}", [P, 2, CH]) for i in range(2)]
        pt_hi = [sb(f"pt_hi{i}", [P, 2, CH, NODES], f32r) for i in range(2)]
        pt_lo = [sb(f"pt_lo{i}", [P, 2, CH, NODES], f32r) for i in range(2)]
        y = [sb(f"y{n}", [P, CH, DIM]) for n in range(2)]
        x1 = sb("x1", [P, CH, DIM])
        h = sb("h", [P, CH, DIM])
        x1_b = [sb(f"x1_b{i}", [P, CH, DIM]) for i in range(2)]
        out_sb = [sb(f"out_sb{i}", [P, CH, DIM]) for i in range(2)]
        bn = [sb(f"bn{n}", [P, CH, 6]) for n in range(3)]
        stats = [sb(f"stats{n}", [P, CH, 2]) for n in range(3)]
        var_eps = [sb(f"var_eps{n}", [P, CH]) for n in range(3)]
        rstd = [sb(f"rstd{n}", [P, CH]) for n in range(3)]
        ln_in, ln_out = (y[0], x1, y[1]), (x1, h, None)

        banks = [ctx.enter_context(nc.psum_tensor(f"bank{i}", [P, 512], f32)) for i in range(8)]
        s_ps, t_ps, m_ps = banks[0:2], banks[2:4], banks[4:8]

        w_loaded = {n: sem(f"w_loaded_{n}") for n in W_NAMES}
        vec_loaded = sem("vec_loaded")
        x_loaded = [sem(f"x_loaded{i}") for i in range(2)]
        adj_loaded = [sem(f"adj_loaded{i}") for i in range(2)]
        out_stored = [sem(f"out_stored{i}") for i in range(2)]
        w_hi_done = sem("w_hi_done")
        w_lo_done = sem("w_lo_done")
        zeros_done = sem("zeros_done")
        ident_zeroed = sem("ident_zeroed")
        consts_done = sem("consts_done")

        dve_held, pool_held = sem("dve_held"), sem("pool_held")

        def by_layer(name):
            return [sem(f"{name}{n}") for n in range(2)]

        s_done = by_layer("s_done")
        t_done = by_layer("t_done")
        pv_done = by_layer("pv_done")
        proj_done = by_layer("proj_done")
        wo_done = by_layer("wo_done")
        xt_done = by_layer("xt_done")
        max_done = by_layer("max_done")
        rsum_done = by_layer("rsum_done")
        pt_lo_done = by_layer("pt_lo_done")
        ot_lo_done = by_layer("ot_lo_done")
        proj_lo_done = by_layer("proj_lo_done")
        xt_lo_done = by_layer("xt_lo_done")
        exp_done = by_layer("exp_done")
        pt_hi_done = by_layer("pt_hi_done")
        ot_hi_done = by_layer("ot_hi_done")
        proj_hi_done = by_layer("proj_hi_done")
        xt_hi_done = by_layer("xt_hi_done")
        ht_done = sem("ht_done")
        y_done = by_layer("y_done")
        probs_done = by_layer("probs_done")
        mask_sel = sem("mask_sel")
        mask_done = by_layer("mask_done")
        xb_done = by_layer("xb_done")
        bn_done = [sem(f"bn_done{n}") for n in range(3)]
        stats_done = [sem(f"stats_done{n}") for n in range(3)]
        var_done = [sem(f"var_done{n}") for n in range(3)]
        rstd_done = [sem(f"rstd_done{n}") for n in range(3)]
        ln_done = [sem(f"ln_done{n}") for n in range(3)]

        FIRST = 2
        LAST = (GRAPHS - 2) // 2

        def iterations(eng, body):
            for t in range(-1, 2 * FIRST):
                body(Step(t=t))
            with eng.Fori(FIRST, LAST) as r:
                for j in range(2):
                    body(Step(r=r, j=j, first=FIRST))
            for t in range(2 * LAST, GRAPHS + 3):
                body(Step(t=t))

        def before(step, k):
            for k in range(k - 1, k - 1 - 4 * SLOTS, -1):
                layer, d, pair = slot_of(k)
                if step.has(d):
                    return layer, d, pair
            return None

        def last_reader(step, n):
            for back in range(5):
                same = [m for m in range(len(USERS)) if m % BANKS == n % BANKS and (back or m < n)]
                for m in reversed(same):
                    name, layer, which, d = USERS[m]
                    d -= back
                    if step.has(d):
                        return {"pv": (ot_lo_done[layer], step.count(PAIRS[layer], d, which + 1)),
                                "proj": (proj_lo_done[layer], step.count(PROJ[layer], d, which + 1)),
                                "wo": (y_done[layer], step.count(1, d, 1)),
                                "xt": (xt_lo_done[0], step.count(1, d, 1)),
                                "ht": (ht_done, step.count(1, d, 1))}[name]
            return None

        def tasks_of(k):
            n = sum(len(BEFORE[i]) + 1 + len(AFTER[i]) for i in range(k))
            m = n + len(BEFORE[k])
            return ([(n + i, u) for i, u in enumerate(BEFORE[k])], m,
                    [(m + 1 + i, u) for i, u in enumerate(AFTER[k])])

        def v_place(v, layer, at, bank):
            if layer:
                return (v[1][:, at, :].rearrange("p (g d) -> p g d", d=P)[:, :, 0:HEAD],
                        bank[:].rearrange("p (g d) -> p g d", d=HEAD))
            return (v[0][:].rearrange("p c (g d) -> p (c g) d", d=P)[:, :, 0:HEAD],
                    bank[:].rearrange("p (g d) -> p g d", d=HEAD))

        block = ctx.enter_context(nc.Block())

        @block.sync
        def _(sp):
            def body(step):
                if step.has(1):
                    par = step.parity(1)
                    if step.has(-1):
                        sp.wait_ge(y_done[0], step.count(1, -1, 1))
                    sp.dma_start(x_in[par][:], x_v[step.graph(1)]).then_inc(x_loaded[par], 16)
                    if step.has(-1):
                        sp.wait_ge(mask_done[0], step.count(1, -1, 1))
                    if step.has(-1):
                        sp.wait_ge(mask_done[1], step.count(1, -1, 1))
                    sp.dma_start(adj_in[par][:], adj_v[step.graph(1)]).then_inc(adj_loaded[par], 16)
                if step.t == -1:
                    sp.dma_start(gamma_sb[:], gamma.rearrange("(c p) -> p c", p=P), allow_slow_non_contiguous=True).then_inc(vec_loaded, 16)
                    sp.dma_start(beta_sb[:], beta.rearrange("(c p) -> p c", p=P), allow_slow_non_contiguous=True).then_inc(vec_loaded, 16)
                    for b_sb, b in zip(bias_sb, (bo0, bo1)):
                        sp.dma_start(b_sb[:], b.rearrange("(a n) -> a n", a=1).broadcast_to([P, DIM])).then_inc(vec_loaded, 16)
                if step.has(-3):
                    par = step.parity(-3)
                    sp.wait_ge(ln_done[2], step.count(1, -3, 1))
                    sp.dma_start(out_v[step.graph(-3)], out_sb[par][:]).then_inc(out_stored[par], 16)

            iterations(sp, body)
            for s in out_stored:
                sp.wait_ge(s, 16 * GRAPHS // 2)

        @block.tensor
        def _(pe):
            def three(ps, a_hi, a_lo, b_hi, b_lo, start, stop):
                nc.tensor.matmul(ps, a_hi, b_hi, start=start, stop=False)
                nc.tensor.matmul(ps, a_hi, b_lo, start=False, stop=False)
                return nc.tensor.matmul(ps, a_lo, b_hi, start=False, stop=stop)

            def scores(step, k):
                layer, d, pair = slot_of(k)
                if not step.has(d):
                    return
                pe.wait_ge(proj_lo_done[layer], step.count(PROJ[layer], d, 2 if pair < 2 else 4))
                if prev := before(step, k):
                    pe.wait_ge(max_done[prev[0]], step.head(prev, 1))
                q, kk = (qk_hi[layer]["q"], qk_lo[layer]["q"]), (qk_hi[layer]["k"], qk_lo[layer]["k"])
                parts = ((0, 0), (0, 1), (1, 0))
                for ic in range(CH):
                    for n, (a, b) in enumerate(parts):
                        for hh in range(2):
                            rows = slice(hh * HEAD, (hh + 1) * HEAD)
                            mm = nc.tensor.matmul(s_ps[hh][:, ic * NODES:(ic + 1) * NODES],
                                                  q[a][rows, pair, ic * P:(ic + 1) * P], kk[b][rows, pair, :],
                                                  start=n == 0, stop=n == 2)
                            if ic == CH - 1 and n == 2:
                                mm.then_inc(s_done[layer], 1)

            def transposes(step, k):
                layer, d, pair = slot_of(k)
                if not step.has(d):
                    return
                for hh in range(2):
                    pe.wait_ge(probs_done[layer], step.head((layer, d, pair), hh))
                    if prev := before(step, k):
                        pe.wait_ge(pt_lo_done[prev[0]], step.head(prev, hh))
                    for jc in range(CH):
                        for ic in range(CH):
                            o = jc * NODES + ic * P
                            mm = nc.tensor.transpose(t_ps[hh][:, o:o + P], probs[k % 2][:, hh, ic, jc * P:(jc + 1) * P],
                                                     ident[:])
                    mm.then_inc(t_done[layer], 1)

            def attend(step, k, n):
                layer, d, pair = slot_of(k)
                if not step.has(d):
                    return
                pe.wait_ge(pt_lo_done[layer], step.head((layer, d, pair), 1))
                pe.wait_ge(proj_lo_done[layer], step.count(PROJ[layer], d, PROJ[layer]))
                if reader := last_reader(step, n):
                    pe.wait_ge(*reader)
                ps = m_ps[n % BANKS][:, 0:NODES]
                for hh in range(2):
                    o = (2 * pair + hh) * P - hh * HEAD
                    for jc in range(CH):
                        mm = three(ps, v_hi[layer][:, jc, o:o + P], v_lo[layer][:, jc, o:o + P],
                                   pt_hi[k % 2][:, hh, jc, :], pt_lo[k % 2][:, hh, jc, :],
                                   hh == 0 and jc == 0, hh == 1 and jc == CH - 1)
                mm.then_inc(pv_done[layer], 1)

            def project(step, layer, which, d, n):
                what, at = (ORDER_L0, ORDER_L1)[layer][which]
                pe.wait_ge(xt_lo_done[layer], step.count(1, d, 1))
                if step.r is None:
                    pe.wait_ge(w_lo_done, 5 if layer else which + 1)
                if reader := last_reader(step, n):
                    pe.wait_ge(*reader)
                a_hi, a_lo = xt_hi[layer], xt_lo[layer]
                name = "qkv1" if layer else what + "0"
                w_at = "qkv".index(what) * INNER[1] if layer else 0
                bank = m_ps[n % BANKS]
                if what == "v":
                    for jc in (at,) if layer else range(CH):
                        ps = bank[:, 0:INNER[1]] if layer else bank[:, jc * INNER[0]:(jc + 1) * INNER[0]]
                        cols, rows = slice(w_at, w_at + INNER[layer]), slice(jc * P, (jc + 1) * P)
                        for c in range(CH):
                            mm = three(ps, a_hi[:, c, rows], a_lo[:, c, rows], w_hi[name][:, c, cols],
                                       w_lo[name][:, c, cols], c == 0, c == CH - 1)
                else:
                    for i in range(2):
                        ps, o = bank[:, i * NODES:(i + 1) * NODES], w_at + (2 * at + i) * P
                        for c in range(CH):
                            mm = three(ps, w_hi[name][:, c, o:o + P], w_lo[name][:, c, o:o + P],
                                       a_hi[:, c, :], a_lo[:, c, :], c == 0, c == CH - 1)
                mm.then_inc(proj_done[layer], 1)

            def output_product(step, layer, d, n):
                pe.wait_ge(ot_lo_done[layer], step.count(PAIRS[layer], d, PAIRS[layer]))
                if step.r is None:
                    pe.wait_ge(w_lo_done, 6 if layer else 4)
                if reader := last_reader(step, n):
                    pe.wait_ge(*reader)
                name = f"o{layer}"
                for ic in range(CH):
                    ps, rows = m_ps[n % BANKS][:, ic * DIM:(ic + 1) * DIM], slice(ic * P, (ic + 1) * P)
                    for c in range(PAIRS[layer]):
                        mm = three(ps, ot_hi[layer][:, c, rows], ot_lo[layer][:, c, rows],
                                   w_hi[name][:, c, :], w_lo[name][:, c, :], c == 0, c == PAIRS[layer] - 1)
                mm.then_inc(wo_done[layer], 1)

            def transpose_rows(step, layer, d, n):
                if layer:
                    src = h
                    pe.wait_ge(ln_done[1], step.count(1, d, 1))
                else:
                    src = x_in[step.parity(d)]
                    pe.wait_ge(x_loaded[step.parity(d)], step.dma(d))
                if reader := last_reader(step, n):
                    pe.wait_ge(*reader)
                for c in range(CH):
                    for ic in range(CH):
                        o = c * NODES + ic * P
                        mm = nc.tensor.transpose(m_ps[n % BANKS][:, o:o + P], src[:, ic, c * P:(c + 1) * P], ident[:])
                mm.then_inc(xt_done[layer], 1)

            def task(step, n, user):
                name, layer, which, d = user
                if not step.has(d):
                    return
                if name == "proj":
                    project(step, layer, which, d, n)
                elif name == "wo":
                    output_product(step, layer, d, n)
                else:
                    transpose_rows(step, layer, d, n)

            pe.wait_ge(consts_done, 1)
            def body(step):
                for k in range(SLOTS):
                    first, pv, last = tasks_of(k)
                    scores(step, k)
                    for n, user in first:
                        task(step, n, user)
                    transposes(step, k - 1)
                    attend(step, k - 2, pv)
                    for n, user in last:
                        task(step, n, user)

            iterations(pe, body)

        @block.scalar
        def _(act):
            for n in W_NAMES:
                act.dma_start(w_raw[n][:], W_DRAM[n].rearrange("(c p) n -> p c n", p=P)).then_inc(w_loaded[n], 16)

            def split_weight(n):
                act.wait_ge(w_loaded[n], 16)
                nc.scalar.activation(w_hi[n][:], w_raw[n][:], ACT.Copy).then_inc(w_hi_done, 1)

            for n in SPLIT_AT["start"]:
                split_weight(n)

            def exponentials(step, k, hh):
                layer, d, pair = slot_of(k)
                if not step.has(d):
                    return
                act.wait_ge(max_done[layer], step.head((layer, d, pair), hh))
                for ic in range(CH):
                    e = nc.scalar.activation(probs[k % 2][:, hh, ic, :], probs[k % 2][:, hh, ic, :], ACT.Exp,
                                             bias=negmax[k % 2][:, hh, ic:ic + 1], scale=-1.0,
                                             accum_out=sums[k % 2][:, hh, ic:ic + 1])
                e.then_inc(exp_done[layer], 1)

            def transposed_hi(step, k):
                layer, d, pair = slot_of(k)
                if not step.has(d):
                    return
                for hh in range(2):
                    act.wait_ge(t_done[layer], step.head((layer, d, pair), hh))
                    nc.scalar.activation(pt_hi[k % 2][:, hh, :, :], t_ps[hh][:].rearrange("p (c i) -> p c i", c=CH),
                                         ACT.Copy).then_inc(pt_hi_done[layer], 1)

            def attended_hi(step, k, n):
                layer, d, pair = slot_of(k)
                if not step.has(d):
                    return
                act.wait_ge(pv_done[layer], step.count(PAIRS[layer], d, pair + 1))
                nc.scalar.activation(ot_hi[layer][:, pair, :], m_ps[n % BANKS][:, 0:NODES],
                                     ACT.Copy).then_inc(ot_hi_done[layer], 1)

            def task(step, n, user):
                name, layer, which, d = user
                if not step.has(d) or name == "wo":
                    return
                bank = m_ps[n % BANKS]
                if name == "proj":
                    act.wait_ge(proj_done[layer], step.count(PROJ[layer], d, which + 1))
                    what, at = (ORDER_L0, ORDER_L1)[layer][which]
                    if what == "v":
                        if step.r is None:
                            act.wait_ge(zeros_done, layer + 1)
                        dst, src = v_place(v_hi, layer, at, bank)
                    else:
                        dst, src = qk_hi[layer][what][:, 2 * at:2 * at + 2, :], bank[:].rearrange("p (c i) -> p c i", c=2)
                    nc.scalar.activation(dst, src, ACT.Copy).then_inc(proj_hi_done[layer], 1)
                elif name == "xt":
                    act.wait_ge(xt_done[0], step.count(1, d, 1))
                    nc.scalar.activation(xt_hi[0][:], bank[:].rearrange("p (c i) -> p c i", c=CH),
                                         ACT.Copy).then_inc(xt_hi_done[0], 1)
                else:
                    if step.r is None:
                        act.wait_ge(vec_loaded, 64)
                    act.wait_ge(xt_done[1], step.count(1, d, 1))
                    if step.has(d - 1):
                        act.wait_ge(xt_lo_done[1], step.count(1, d - 1, 1))
                    for c in range(CH):
                        a = nc.scalar.activation(ht[:, c, :], bank[:, c * NODES:(c + 1) * NODES], ACT.Identity,
                                                 bias=beta_sb[:, c:c + 1], scale=gamma_sb[:, c:c + 1])
                    a.then_inc(ht_done, 1)

            def body(step):
                for k in range(SLOTS):
                    first, pv, last = tasks_of(k)
                    exponentials(step, k, 0)
                    for n, user in first:
                        task(step, n, user)
                    exponentials(step, k, 1)
                    transposed_hi(step, k - 1)
                    attended_hi(step, k - 2, pv)
                    for n, user in last:
                        task(step, n, user)
                    if step.t is not None:
                        for n in SPLIT_AT.get((step.t, k), ()):
                            split_weight(n)

            iterations(act, body)

        @block.vector
        def _(dve):
            def split_weight(n):
                dve.wait_ge(w_hi_done, W_NAMES.index(n) + 1)
                nc.vector.tensor_tensor(w_lo[n][:], w_raw[n][:], w_hi[n][:].bitcast(f32),
                                        ALU.subtract).then_inc(w_lo_done, 1)

            for n in SPLIT_AT["start"]:
                split_weight(n)

            def maxima(step, k):
                layer, d, pair = slot_of(k)
                if not step.has(d):
                    return
                for hh in range(2):
                    if hh == 0:
                        dve.wait_ge(mask_done[layer], step.count(1, d, 1))
                    dve.wait_ge(s_done[layer], step.head((layer, d, pair), hh))
                    step.hold(dve, dve_held)
                    for ic in range(CH):
                        m = nc.vector.tensor_tensor_reduce(
                            out=probs[k % 2][:, hh, ic, :], in0=s_ps[hh][:, ic * NODES:(ic + 1) * NODES],
                            in1=mask[layer][step.parity(d)][:, ic, :], scale=-SCALE, scalar=LARGEST,
                            op0=ALU.add, op1=ALU.min, accum_out=negmax[k % 2][:, hh, ic:ic + 1])
                    m.then_inc(max_done[layer], 1)

            def reciprocal_sums(step, k, hh):
                layer, d, pair = slot_of(k)
                if not step.has(d):
                    return
                dve.wait_ge(exp_done[layer], step.head((layer, d, pair), hh))
                nc.vector.reciprocal(rsums[k % 2][:, hh, :], sums[k % 2][:, hh, :]).then_inc(rsum_done[layer], 1)

            def transposed_lo(step, k, hh):
                layer, d, pair = slot_of(k)
                if not step.has(d):
                    return
                dve.wait_ge(pt_hi_done[layer], step.head((layer, d, pair), hh))
                nc.vector.tensor_tensor(pt_lo[k % 2][:, hh, :, :], t_ps[hh][:].rearrange("p (c i) -> p c i", c=CH),
                                        pt_hi[k % 2][:, hh, :, :].bitcast(f32), ALU.subtract).then_inc(pt_lo_done[layer], 1)

            def attended_lo(step, k, n):
                layer, d, pair = slot_of(k)
                if not step.has(d):
                    return
                dve.wait_ge(ot_hi_done[layer], step.count(PAIRS[layer], d, pair + 1))
                nc.vector.tensor_tensor(ot_lo[layer][:, pair, :], m_ps[n % BANKS][:, 0:NODES],
                                        ot_hi[layer][:, pair, :].bitcast(f32), ALU.subtract).then_inc(ot_lo_done[layer], 1)

            def statistics(step, w, d):
                for ic in range(CH):
                    b = nc.vector.bn_stats(bn[w][:, ic, :], ln_in[w][:, ic, :])
                b.then_inc(bn_done[w], 1)
                dve.wait_ge(bn_done[w], step.count(1, d, 1))
                step.hold(dve, dve_held)
                for ic in range(CH):
                    b = nc.vector.bn_aggr(stats[w][:, ic, :], bn[w][:, ic, :])
                b.then_inc(stats_done[w], 1)

            def normalise(step, w, d):
                if not step.has(d):
                    return
                dst = ln_out[w] if w < 2 else out_sb[step.parity(d)]
                if w == 0:
                    if step.has(d - 1):
                        dve.wait_ge(xb_done[1], step.count(1, d - 1, 1))
                if w == 1:
                    if step.has(d - 1):
                        dve.wait_ge(xt_done[1], step.count(1, d - 1, 1))
                if w == 2:
                    if step.has(d - 2):
                        dve.wait_ge(out_stored[step.parity(d)], step.dma(d - 2))
                dve.wait_ge(rstd_done[w], step.count(1, d, 1))
                for ic in range(CH):
                    o = nc.vector.tensor_scalar(dst[:, ic, :], ln_in[w][:, ic, :], stats[w][:, ic, 0:1],
                                                rstd[w][:, ic:ic + 1], ALU.subtract, ALU.mult)
                o.then_inc(ln_done[w], 1)

            def task(step, n, user):
                name, layer, which, d = user
                if not step.has(d):
                    return
                bank = m_ps[n % BANKS]
                if name == "proj":
                    dve.wait_ge(proj_hi_done[layer], step.count(PROJ[layer], d, which + 1))
                    what, at = (ORDER_L0, ORDER_L1)[layer][which]
                    if what == "v":
                        (dst, src), (hi, _) = v_place(v_lo, layer, at, bank), v_place(v_hi, layer, at, bank)
                    else:
                        dst, src = qk_lo[layer][what][:, 2 * at:2 * at + 2, :], bank[:].rearrange("p (c i) -> p c i", c=2)
                        hi = qk_hi[layer][what][:, 2 * at:2 * at + 2, :]
                    nc.vector.tensor_tensor(dst, src, hi.bitcast(f32), ALU.subtract).then_inc(proj_lo_done[layer], 1)
                elif name == "xt":
                    dve.wait_ge(xt_hi_done[0], step.count(1, d, 1))
                    nc.vector.tensor_tensor(xt_lo[0][:], bank[:].rearrange("p (c i) -> p c i", c=CH),
                                            xt_hi[0][:].bitcast(f32), ALU.subtract).then_inc(xt_lo_done[0], 1)
                elif name == "ht":
                    dve.wait_ge(ht_done, step.count(1, d, 1))
                    nc.vector.tensor_copy(xt_hi[1][:], ht[:]).then_inc(xt_hi_done[1], 1)
                else:
                    res = x1_b[step.parity(d)] if layer else x_in[step.parity(d)]
                    dve.wait_ge(xb_done[layer], step.count(1, d, 1))
                    dve.wait_ge(wo_done[layer], step.count(1, d, 1))
                    nc.vector.tensor_tensor(y[layer][:], bank[:].rearrange("p (c i) -> p c i", c=CH), res[:],
                                            ALU.add).then_inc(y_done[layer], 1)
                    dve.wait_ge(y_done[layer], step.count(1, d, 1))
                    statistics(step, 2 * layer, d)

            def body(step):
                for k in range(SLOTS):
                    first, pv, last = tasks_of(k)
                    maxima(step, k)
                    if k == 0:
                        normalise(step, 1, -1)
                        normalise(step, 2, -3)
                    if k == 5 and step.has(0):
                        normalise(step, 0, 0)
                        dve.wait_ge(ln_done[0], step.count(1, 0, 1))
                        statistics(step, 1, 0)
                    for n, user in first:
                        task(step, n, user)
                    reciprocal_sums(step, k, 0)
                    reciprocal_sums(step, k, 1)
                    transposed_lo(step, k - 1, 0)
                    transposed_lo(step, k - 1, 1)
                    attended_lo(step, k - 2, pv)
                    for n, user in last:
                        task(step, n, user)
                    if step.t is not None:
                        for n in SPLIT_AT.get((step.t, k), ()):
                            split_weight(n)

            iterations(dve, body)

        @block.gpsimd
        def _(pool):
            nc.gpsimd.memset(minus_half[:], -0.5)
            nc.gpsimd.memset(ident[:], 0.0).then_inc(ident_zeroed, 1)
            pool.wait_ge(ident_zeroed, 1)
            nc.gpsimd.affine_select(out=ident[:], in_=ident[:], compare_op=ALU.not_equal, fill=1.0, base=0,
                                    pattern=[[-1, P]], channel_multiplier=1).then_inc(consts_done, 1)
            pool.wait_ge(consts_done, 1)
            for hi, lo in zip(v_hi, v_lo):
                nc.gpsimd.memset(hi[:].bitcast(f32), 0.0)
                nc.gpsimd.memset(lo[:].bitcast(f32), 0.0).then_inc(zeros_done, 1)
            pool.wait_ge(vec_loaded, 64)

            def probabilities(step, k, hh):
                layer, d, pair = slot_of(k)
                if not step.has(d):
                    return
                pool.wait_ge(rsum_done[layer], step.head((layer, d, pair), hh))
                step.hold(pool, pool_held)
                for ic in range(CH):
                    e = probs[k % 2][:, hh, ic, :]
                    o = nc.gpsimd.tensor_scalar(e, e, rsums[k % 2][:, hh, ic:ic + 1], 1.0, ALU.mult, ALU.mult)
                o.then_inc(probs_done[layer], 1)

            def reciprocal_std(step, w, d):
                if not step.has(d):
                    return
                pool.wait_ge(stats_done[w], step.count(1, d, 1))
                step.hold(pool, pool_held)
                nc.gpsimd.tensor_scalar(var_eps[w][:], stats[w][:, :, 1], EPS, 1.0, ALU.add,
                                        ALU.mult).then_inc(var_done[w], 1)
                pool.wait_ge(var_done[w], step.count(1, d, 1))
                nc.gpsimd.tensor_tensor(rstd[w][:], var_eps[w][:], minus_half[:], ALU.pow).then_inc(rstd_done[w], 1)

            def make_mask(step, layer, d):
                if not step.has(d):
                    return
                m = mask[layer][step.parity(d)]
                pool.wait_ge(adj_loaded[step.parity(d)], step.dma(d))
                if step.has(d - 2):
                    pool.wait_ge(max_done[layer], step.count(HEADS[layer], d - 2, HEADS[layer]))
                step.hold(pool, pool_held)
                o = nc.gpsimd.tensor_scalar(m[:], adj_in[step.parity(d)][:], -1.0, (MASKED0, MASKED1)[layer],
                                            ALU.add, ALU.mult)
                if layer == 0:
                    o.then_inc(mask_done[0], 1)
                    return
                o.then_inc(mask_sel, 1)
                pool.wait_ge(mask_sel, step.count(1, d, 1))
                step.hold(pool, pool_held)
                nc.gpsimd.affine_select(out=m[:], in_=m[:], compare_op=ALU.not_equal, fill=0.0, base=0,
                                        pattern=[[P, CH], [-1, NODES]], channel_multiplier=1).then_inc(mask_done[1], 1)

            def add_bias(step, layer, d):
                if not step.has(d):
                    return
                if layer:
                    src, dst = x1, x1_b[step.parity(d)]
                    pool.wait_ge(ln_done[0], step.count(1, d, 1))
                    if step.has(d - 2):
                        pool.wait_ge(y_done[1], step.count(1, d - 2, 1))
                else:
                    src = dst = x_in[step.parity(d)]
                    pool.wait_ge(xt_done[0], step.count(1, d, 1))
                for ic in range(CH):
                    o = nc.gpsimd.tensor_tensor(dst[:, ic, :], src[:, ic, :], bias_sb[layer][:], ALU.add)
                o.then_inc(xb_done[layer], 1)

            def ht_lo(step, d):
                if not step.has(d):
                    return
                pool.wait_ge(xt_hi_done[1], step.count(1, d, 1))
                nc.gpsimd.tensor_tensor(xt_lo[1][:], ht[:], xt_hi[1][:].bitcast(f32),
                                        ALU.subtract).then_inc(xt_lo_done[1], 1)

            def body(step):
                for k in range(SLOTS):
                    if k == 1:
                        ht_lo(step, -1)
                    if k == 4:
                        reciprocal_std(step, 0, 0)
                    if k == 5:
                        reciprocal_std(step, 1, 0)
                        reciprocal_std(step, 2, -2)
                    probabilities(step, k, 0)
                    probabilities(step, k, 1)
                    if k == 1:
                        make_mask(step, 0, 1)
                    if k == 2:
                        add_bias(step, 0, 0)
                    if k == 3:
                        make_mask(step, 1, 0)
                    if k == 5:
                        add_bias(step, 1, 0)

            iterations(pool, body)


_INS = ["x", "adj", "L0_gnn_Wq", "L0_gnn_Wk", "L0_gnn_Wv", "L0_gnn_Wo", "L0_gnn_bo", "L1_gnn_gamma", "L1_gnn_beta",
        "L1_gnn_w_qkv", "L1_gnn_w_out", "L1_gnn_b_out"]
_TRANSPOSED = ("L1_gnn_w_qkv", "L1_gnn_w_out")


def kernel(**inputs):
    import concourse.bacc as _bacc
    from concourse.bass_utils import run_bass_kernel_spmd as _run

    nc = _bacc.Bacc("TRN2", target_bir_lowering=False, num_devices=1)
    arrays, args = {}, []
    for name in _INS:
        a = np.asarray(inputs[name])
        if name in _TRANSPOSED:
            a = a.T
        a = np.ascontiguousarray(a)
        arrays[f"in_{name}"] = a
        args.append(nc.dram_tensor(f"in_{name}", a.shape, mybir.dt.from_np(a.dtype), kind="ExternalInput").ap())
    out = nc.dram_tensor("out_0", (GRAPHS, NODES, DIM), mybir.dt.float32, kind="ExternalOutput").ap()
    build(nc, *args, out)
    r = _run(nc, [arrays], core_ids=[0])
    return r.results[0]["out_0"]
```

```python
from contextlib import ExitStack

import numpy as np

import concourse.bass as bass
from concourse import mybir

GRAPHS, NODES, DIM = 32, 256, 256
P = 128
CH = NODES // P
HEAD = 64
HEADS = (4, 8)
PAIRS = (2, 4)
SLOTS = PAIRS[0] + PAIRS[1]
INNER = (HEADS[0] * HEAD, HEADS[1] * HEAD)
PROJ = (3, 6)
EPS = 1e-5
SCALE = HEAD ** -0.5
MASKED0 = float(np.finfo(np.float32).max)
MASKED1 = 1e9 / SCALE
LARGEST = 3.0e38

SLOT = ((0, 0, 0), (0, 0, 1), (1, -2, 3), (1, -1, 0), (1, -1, 1), (1, -1, 2))


def slot_of(k):
    layer, d, pair = SLOT[k % SLOTS]
    return layer, d + k // SLOTS, pair


PE_ORDER = (
    ("scores", 0), ("xt", 0, 0, 1), ("transpose", -1, 0), ("transpose", -1, 1), ("pv", -2), ("scores", 1),
    ("ht", 1, 0, -1), ("proj", 0, 0, 1), ("pv", -1), ("transpose", 0, 0), ("transpose", 0, 1), ("scores", 2),
    ("proj", 1, 0, -1), ("proj", 1, 1, -1), ("transpose", 1, 0), ("proj", 1, 2, -1), ("transpose", 1, 1),
    ("pv", 0), ("scores", 3), ("transpose", 2, 0), ("transpose", 2, 1), ("pv", 1), ("proj", 1, 3, -1),
    ("scores", 4), ("transpose", 3, 0), ("proj", 0, 1, 1), ("pv", 2), ("wo", 0, 0, 0), ("transpose", 3, 1),
    ("scores", 5), ("proj", 1, 4, -1), ("proj", 0, 2, 1), ("proj", 1, 5, -1), ("transpose", 4, 0),
    ("wo", 1, 0, -2), ("transpose", 4, 1), ("pv", 3),
)

ACT_ORDER = (
    ("pt", -1, 0), ("weight", -1, "q0"), ("weight", -1, "k0"), ("xt", 0, 0, 1), ("exp", 0, 0), ("pt", -1, 1),
    ("exp", 0, 1), ("ht", 1, 0, -1), ("half", -2), ("exp", 1, 0), ("pt", 0, 0), ("half", -1), ("pt", 0, 1),
    ("exp", 1, 1), ("ot", -2), ("proj", 0, 0, 1), ("exp", 2, 0), ("proj", 1, 0, -1), ("proj", 1, 1, -1),
    ("pt", 1, 0), ("weight", 0, "qkv1"), ("exp", 2, 1), ("proj", 1, 2, -1), ("pt", 1, 1), ("half", 0),
    ("weight", 0, "o1"), ("weight", -1, "v0"), ("ot", -1), ("pt", 2, 0), ("exp", 3, 0), ("ot", 0), ("half", 1),
    ("pt", 2, 1), ("weight", -1, "o0"), ("exp", 3, 1), ("ot", 1), ("pt", 3, 0), ("proj", 1, 3, -1),
    ("proj", 0, 1, 1), ("half", 2), ("exp", 4, 0), ("pt", 3, 1), ("ot", 2), ("exp", 4, 1), ("proj", 1, 4, -1),
    ("exp", 5, 0), ("proj", 0, 2, 1), ("proj", 1, 5, -1), ("exp", 5, 1), ("pt", 4, 0), ("pt", 4, 1),
    ("half", 3), ("ot", 3),
)

DVE_ORDER = (
    ("max", 0, 0), ("max", 0, 1), ("weight", -1, "q0"), ("norm", 1, -1), ("xt", 0, 0, 1), ("rsum", 0, 0),
    ("pt", -1, 0), ("pt", -1, 1), ("rsum", 0, 1), ("max", 1, 0), ("ht", 1, 0, -1), ("max", 1, 1), ("sum", -2),
    ("norm", 2, -3), ("sum", -1), ("rsum", 1, 0), ("max", 2, 0), ("pt", 0, 0), ("max", 2, 1),
    ("weight", -1, "k0"), ("rsum", 1, 1), ("pt", 0, 1), ("rsum", 2, 0), ("proj", 0, 0, 1), ("proj", 1, 0, -1),
    ("proj", 1, 1, -1), ("pt", 1, 0), ("rsum", 2, 1), ("proj", 1, 2, -1), ("weight", -1, "v0"), ("pt", 1, 1),
    ("max", 3, 0), ("sum", 0), ("max", 3, 1), ("rsum", 3, 0), ("pt", 2, 0), ("sum", 1), ("pt", 2, 1),
    ("weight", 0, "qkv1"), ("max", 4, 0), ("rsum", 3, 1), ("max", 4, 1), ("pt", 3, 0), ("weight", -1, "o0"),
    ("proj", 1, 3, -1), ("proj", 0, 1, 1), ("sum", 2), ("wo", 0, 0, 0), ("rsum", 4, 0), ("stats", 0, 0),
    ("max", 5, 0), ("weight", 0, "o1"), ("pt", 3, 1), ("max", 5, 1), ("norm", 0, 0), ("proj", 1, 4, -1),
    ("rsum", 4, 1), ("stats", 1, 0), ("proj", 1, 5, -1), ("proj", 0, 2, 1), ("rsum", 5, 0), ("pt", 4, 0),
    ("wo", 1, 0, -2), ("rsum", 5, 1), ("stats", 2, -2), ("pt", 4, 1), ("sum", 3),
)

POOL_ORDER = (
    ("probs", 0, 0), ("probs", 0, 1), ("ht", -1), ("bias", 0, 0), ("probs", 1, 0), ("probs", 1, 1),
    ("probs", 2, 0), ("probs", 2, 1), ("ot", -2), ("ot", -1), ("mask", 0, 1), ("probs", 3, 0), ("ot", 0),
    ("ot", 1), ("probs", 3, 1), ("probs", 4, 0), ("ot", 2), ("rstd", 0, 0), ("probs", 4, 1), ("mask", 1, 0),
    ("probs", 5, 0), ("probs", 5, 1), ("rstd", 1, 0), ("bias", 1, 0), ("rstd", 2, -2), ("ot", 3),
)

BANK = (1, 3, 2, 0, 1, 2, 3, 1, 2, 0, 3, 2, 1, 0, 2, 3, 0, 1, 2)

def bank_users():
    return [("pv", *slot_of(k[0])[::2], slot_of(k[0])[1]) if name == "pv" else (name, *k)
            for name, *k in PE_ORDER if name not in ("scores", "transpose")]


USERS = bank_users()
ORDER_L1 = ("q", 0), ("k", 0), ("q", 1), ("k", 1), ("v", 0), ("v", 1)
ORDER_L0 = ("q", 0), ("k", 0), ("v", 0)


class Step:

    def __init__(self, t=None, r=None, j=None, first=None):
        self.t, self.r, self.j = t, r, j
        self.first = first

    def has(self, d):
        return self.r is not None or 0 <= self.t + d < GRAPHS

    def parity(self, d):
        return ((self.t if self.r is None else self.j) + d) % 2

    def graph(self, d):
        return self.t + d if self.r is None else self.r * 2 + (self.j + d)

    def count(self, per, d, n):
        if self.r is None:
            return per * (self.t + d) + n
        assert 2 * per * self.first + per * (self.j + d) + n > 0
        return self.r * (2 * per) + (per * (self.j + d) + n)

    def head(self, unit, hh):
        layer, d, pair = unit
        return self.count(HEADS[layer], d, 2 * pair + hh + 1)

    def dma(self, d):
        if self.r is None:
            return 16 * ((self.t + d) // 2 + 1)
        return self.r * 16 + 16 * ((self.j + d) // 2 + 1)

    def hold(self, eng, held):
        if self.r is not None:
            eng.sem_inc(held, 1)


def build(nc, x, adj, wq0, wk0, wv0, wo0, bo0, gamma, beta, wqkv1, wo1, bo1, out):
    f32, f32r, u8 = mybir.dt.float32, mybir.dt.float32r, mybir.dt.uint8
    ALU, ACT = mybir.AluOpType, mybir.ActivationFunctionType

    x_v = x.rearrange("b (c p) e -> b p c e", p=P)
    adj_v = adj.rearrange("b (c p) j -> b p c j", p=P)
    out_v = out.rearrange("b (c p) e -> b p c e", p=P)

    ctx = ExitStack()
    with ctx:
        def sb(name, shape, dt=f32):
            return ctx.enter_context(nc.sbuf_tensor(name, shape, dt))

        def sem(name):
            return ctx.enter_context(nc.semaphore(name))

        W_NAMES = ("q0", "k0", "v0", "o0", "qkv1", "o1")
        W_SHAPE = {"q0": (CH, INNER[0]), "k0": (CH, INNER[0]), "v0": (CH, INNER[0]), "o0": (INNER[0] // P, DIM),
                   "qkv1": (CH, 3 * INNER[1]), "o1": (INNER[1] // P, DIM)}
        W_DRAM = {"q0": wq0, "k0": wk0, "v0": wv0, "o0": wo0, "qkv1": wqkv1, "o1": wo1}
        w_raw = {n: sb(f"w_raw_{n}", [P, *W_SHAPE[n]]) for n in W_NAMES}
        w_hi = {n: sb(f"w_hi_{n}", [P, *W_SHAPE[n]], f32r) for n in W_NAMES}
        w_lo = {n: sb(f"w_lo_{n}", [P, *W_SHAPE[n]], f32r) for n in W_NAMES}
        ident = sb("ident", [P, P])
        minus_half = sb("minus_half", [P, CH])
        gamma_sb = sb("gamma_sb", [P, CH])
        beta_sb = sb("beta_sb", [P, CH])
        bias_sb = [sb(f"bias_sb{n}", [P, DIM]) for n in range(2)]

        x_in = [sb(f"x_in{i}", [P, CH, DIM]) for i in range(2)]
        adj_in = [sb(f"adj_in{i}", [P, CH, NODES], u8) for i in range(2)]
        mask = [[sb(f"mask{n}_{i}", [P, CH, NODES]) for i in range(2)] for n in range(2)]
        xt_hi = [sb(f"xt_hi{n}", [P, CH, NODES], f32r) for n in range(2)]
        xt_lo = [sb(f"xt_lo{n}", [P, CH, NODES], f32r) for n in range(2)]
        ht = sb("ht", [P, CH, NODES])
        qk_hi = [{c: sb(f"{c}_hi{n}", [P, PAIRS[n], NODES], f32r) for c in "qk"} for n in range(2)]
        qk_lo = [{c: sb(f"{c}_lo{n}", [P, PAIRS[n], NODES], f32r) for c in "qk"} for n in range(2)]
        v = [sb(f"v{n}", [P, CH, HEADS[n] * P], f32r) for n in range(2)]
        ot_hi = [sb(f"ot_hi{n}", [P, PAIRS[n], NODES], f32r) for n in range(2)]
        ot_lo = [sb(f"ot_lo{n}", [P, PAIRS[n], NODES], f32r) for n in range(2)]
        half = [sb(f"half{i}", [P, NODES]) for i in range(2)]
        ot = [sb(f"ot{i}", [P, NODES]) for i in range(2)]
        probs = [sb(f"probs{i}", [P, 2, CH, NODES]) for i in range(2)]
        negmax = [sb(f"negmax{i}", [P, 2, CH]) for i in range(2)]
        sums = [sb(f"sums{i}", [P, 2, CH]) for i in range(2)]
        rsums = [sb(f"rsums{i}", [P, 2, CH]) for i in range(2)]
        pt_hi = [sb(f"pt_hi{i}", [P, 2, CH, NODES], f32r) for i in range(2)]
        pt_lo = [sb(f"pt_lo{i}", [P, 2, CH, NODES], f32r) for i in range(2)]
        y = [sb(f"y{n}", [P, CH, DIM]) for n in range(2)]
        x1 = sb("x1", [P, CH, DIM])
        h = sb("h", [P, CH, DIM])
        x1_b = [sb(f"x1_b{i}", [P, CH, DIM]) for i in range(2)]
        out_sb = [sb(f"out_sb{i}", [P, CH, DIM]) for i in range(2)]
        bn = [sb(f"bn{n}", [P, CH, 6]) for n in range(3)]
        stats = [sb(f"stats{n}", [P, CH, 2]) for n in range(3)]
        var_eps = [sb(f"var_eps{n}", [P, CH]) for n in range(3)]
        rstd = [sb(f"rstd{n}", [P, CH]) for n in range(3)]
        ln_in, ln_out = (y[0], x1, y[1]), (x1, h, None)

        banks = [ctx.enter_context(nc.psum_tensor(f"bank{i}", [P, 512], f32)) for i in range(8)]
        s_ps, t_ps, m_ps = banks[0:2], banks[2:4], banks[4:8]

        w_loaded = {n: sem(f"w_loaded_{n}") for n in W_NAMES}
        vec_loaded = sem("vec_loaded")
        x_loaded = [sem(f"x_loaded{i}") for i in range(2)]
        adj_loaded = [sem(f"adj_loaded{i}") for i in range(2)]
        out_stored = [sem(f"out_stored{i}") for i in range(2)]
        w_hi_done = sem("w_hi_done")
        w_lo_done = sem("w_lo_done")
        ident_zeroed = sem("ident_zeroed")
        consts_done = sem("consts_done")

        dve_held, pool_held = sem("dve_held"), sem("pool_held")

        def by_layer(name):
            return [sem(f"{name}{n}") for n in range(2)]

        s_done = by_layer("s_done")
        t_done = by_layer("t_done")
        pv_done = by_layer("pv_done")
        proj_done = by_layer("proj_done")
        wo_done = by_layer("wo_done")
        xt_done = by_layer("xt_done")
        max_done = by_layer("max_done")
        rsum_done = by_layer("rsum_done")
        pt_lo_done = by_layer("pt_lo_done")
        half_done = by_layer("half_done")
        ot_done = by_layer("ot_done")
        ot_lo_done = by_layer("ot_lo_done")
        proj_lo_done = by_layer("proj_lo_done")
        xt_lo_done = by_layer("xt_lo_done")
        exp_done = by_layer("exp_done")
        pt_hi_done = by_layer("pt_hi_done")
        ot_hi_done = by_layer("ot_hi_done")
        proj_hi_done = by_layer("proj_hi_done")
        xt_hi_done = by_layer("xt_hi_done")
        ht_done = sem("ht_done")
        y_done = by_layer("y_done")
        probs_done = by_layer("probs_done")
        mask_sel = sem("mask_sel")
        mask_done = by_layer("mask_done")
        xb_done = by_layer("xb_done")
        bn_done = [sem(f"bn_done{n}") for n in range(3)]
        stats_done = [sem(f"stats_done{n}") for n in range(3)]
        var_done = [sem(f"var_done{n}") for n in range(3)]
        rstd_done = [sem(f"rstd_done{n}") for n in range(3)]
        ln_done = [sem(f"ln_done{n}") for n in range(3)]

        FIRST = 2
        LAST = (GRAPHS - 2) // 2

        def iterations(eng, body):
            for t in range(-1, 2 * FIRST):
                body(Step(t=t))
            with eng.Fori(FIRST, LAST) as r:
                for j in range(2):
                    body(Step(r=r, j=j, first=FIRST))
            for t in range(2 * LAST, GRAPHS + 3):
                body(Step(t=t))

        def before(step, k, by=1):
            for k in range(k - by, k - 4 * SLOTS, -by):
                layer, d, pair = slot_of(k)
                if step.has(d):
                    return layer, d, pair
            return None

        def last_reader(step, n):
            for back in range(5):
                same = [m for m in range(len(USERS)) if BANK[m] == BANK[n] and (back or m < n)]
                for m in reversed(same):
                    name, layer, which, d = USERS[m]
                    d -= back
                    if step.has(d):
                        return {"pv": (ot_done[layer], step.count(PAIRS[layer], d, which + 1), d),
                                "proj": (proj_lo_done[layer], step.count(PROJ[layer], d, which + 1), d),
                                "wo": (y_done[layer], step.count(1, d, 1), d),
                                "xt": (xt_lo_done[0], step.count(1, d, 1), d),
                                "ht": (ht_done, step.count(1, d, 1), d)}[name]
            return None

        def bank_of(user):
            if user[0] == "pv":
                layer, d, pair = slot_of(user[1])
                user = ("pv", layer, pair, d)
            return USERS.index(user)

        def v_place(layer, at, bank, lo):
            chunks = v[1][:, at, :] if layer else v[0][:].rearrange("p c n -> p (c n)")
            quarters = chunks.rearrange("p (g f d) -> p g f d", f=4, d=HEAD)
            return (quarters[:, :, 1:3, :] if lo else quarters[:, :, 0:4:3, :],
                    bank[:].rearrange("p (g f d) -> p g f d", f=2, d=HEAD))

        block = ctx.enter_context(nc.Block())

        @block.sync
        def _(sp):
            def load_weights(names):
                for n in names:
                    sp.dma_start(w_raw[n][:], W_DRAM[n].rearrange("(c p) n -> p c n", p=P)).then_inc(w_loaded[n], 16)

            def body(step):
                if step.has(1):
                    par = step.parity(1)
                    if step.has(-1):
                        sp.wait_ge(y_done[0], step.count(1, -1, 1))
                    sp.dma_start(x_in[par][:], x_v[step.graph(1)]).then_inc(x_loaded[par], 16)
                    if step.t == -1:
                        load_weights(("q0", "k0"))
                    if step.has(-1):
                        sp.wait_ge(mask_done[0], step.count(1, -1, 1))
                    if step.has(-1):
                        sp.wait_ge(mask_done[1], step.count(1, -1, 1))
                    sp.dma_start(adj_in[par][:], adj_v[step.graph(1)]).then_inc(adj_loaded[par], 16)
                if step.t == -1:
                    load_weights(("v0",))
                if step.t == 0:
                    load_weights(("o0", "qkv1", "o1"))
                    sp.dma_start(gamma_sb[:], gamma.rearrange("(c p) -> p c", p=P), allow_slow_non_contiguous=True).then_inc(vec_loaded, 16)
                    sp.dma_start(beta_sb[:], beta.rearrange("(c p) -> p c", p=P), allow_slow_non_contiguous=True).then_inc(vec_loaded, 16)
                    for b_sb, b in zip(bias_sb, (bo0, bo1)):
                        sp.dma_start(b_sb[:], b.rearrange("(a n) -> a n", a=1).broadcast_to([P, DIM])).then_inc(vec_loaded, 16)
                if step.has(-3):
                    par = step.parity(-3)
                    sp.wait_ge(ln_done[2], step.count(1, -3, 1))
                    sp.dma_start(out_v[step.graph(-3)], out_sb[par][:]).then_inc(out_stored[par], 16)

            iterations(sp, body)
            for s in out_stored:
                sp.wait_ge(s, 16 * GRAPHS // 2)

        @block.tensor
        def _(pe):
            def three(ps, a_hi, a_lo, b_hi, b_lo, start, stop):
                nc.tensor.matmul(ps, a_hi, b_hi, start=start, stop=False)
                nc.tensor.matmul(ps, a_hi, b_lo, start=False, stop=False)
                return nc.tensor.matmul(ps, a_lo, b_hi, start=False, stop=stop)

            def scores(step, k):
                layer, d, pair = slot_of(k)
                if not step.has(d):
                    return
                pe.wait_ge(proj_lo_done[layer], step.count(PROJ[layer], d, 2 if pair < 2 else 4))
                if prev := before(step, k):
                    pe.wait_ge(max_done[prev[0]], step.head(prev, 1))
                q, kk = (qk_hi[layer]["q"], qk_lo[layer]["q"]), (qk_hi[layer]["k"], qk_lo[layer]["k"])
                parts = ((0, 0), (0, 1), (1, 0))
                for ic in range(CH):
                    for n, (a, b) in enumerate(parts):
                        for hh in range(2):
                            rows = slice(hh * HEAD, (hh + 1) * HEAD)
                            mm = nc.tensor.matmul(s_ps[hh][:, ic * NODES:(ic + 1) * NODES],
                                                  q[a][rows, pair, ic * P:(ic + 1) * P], kk[b][rows, pair, :],
                                                  start=n == 0, stop=n == 2)
                            if ic == CH - 1 and n == 2:
                                mm.then_inc(s_done[layer], 1)

            def transposes(step, k, hh):
                layer, d, pair = slot_of(k)
                if not step.has(d):
                    return
                pe.wait_ge(probs_done[layer], step.head((layer, d, pair), hh))
                if prev := before(step, k):
                    pe.wait_ge(pt_lo_done[prev[0]], step.head(prev, hh))
                for jc in range(CH):
                    for ic in range(CH):
                        o = jc * NODES + ic * P
                        mm = nc.tensor.transpose(t_ps[hh][:, o:o + P], probs[k % 2][:, hh, ic, jc * P:(jc + 1) * P],
                                                 ident[:])
                mm.then_inc(t_done[layer], 1)

            def attend(step, k, n):
                layer, d, pair = slot_of(k)
                if not step.has(d):
                    return
                pe.wait_ge(pt_lo_done[layer], step.head((layer, d, pair), 1))
                reader = last_reader(step, n)
                same = reader is not None and reader[0] is proj_lo_done[layer]
                if not (same and reader[2] > d):
                    pe.wait_ge(proj_lo_done[layer], step.count(PROJ[layer], d, PROJ[layer]))
                if reader and not (same and reader[2] <= d):
                    pe.wait_ge(reader[0], reader[1])
                for hh in range(2):
                    ps, o = m_ps[BANK[n]][:, hh * NODES:(hh + 1) * NODES], (2 * pair + hh) * P
                    for jc in range(CH):
                        for part in (pt_hi, pt_lo):
                            mm = nc.tensor.matmul(ps, v[layer][:, jc, o:o + P], part[k % 2][:, hh, jc, :],
                                                  start=jc == 0 and part is pt_hi,
                                                  stop=jc == CH - 1 and part is pt_lo)
                mm.then_inc(pv_done[layer], 1)

            def project(step, layer, which, d, n):
                what, at = (ORDER_L0, ORDER_L1)[layer][which]
                pe.wait_ge(xt_lo_done[layer], step.count(1, d, 1))
                if step.r is None:
                    pe.wait_ge(w_lo_done, 5 if layer else which + 1)
                if reader := last_reader(step, n):
                    pe.wait_ge(reader[0], reader[1])
                a_hi, a_lo = xt_hi[layer], xt_lo[layer]
                name = "qkv1" if layer else what + "0"
                w_at = "qkv".index(what) * INNER[1] if layer else 0
                bank = m_ps[BANK[n]]
                if what == "v":
                    for jc in (at,) if layer else range(CH):
                        ps = bank[:, 0:INNER[1]] if layer else bank[:, jc * INNER[0]:(jc + 1) * INNER[0]]
                        cols, rows = slice(w_at, w_at + INNER[layer]), slice(jc * P, (jc + 1) * P)
                        for c in range(CH):
                            mm = three(ps, a_hi[:, c, rows], a_lo[:, c, rows], w_hi[name][:, c, cols],
                                       w_lo[name][:, c, cols], c == 0, c == CH - 1)
                else:
                    for i in range(2):
                        ps, o = bank[:, i * NODES:(i + 1) * NODES], w_at + (2 * at + i) * P
                        for c in range(CH):
                            mm = three(ps, w_hi[name][:, c, o:o + P], w_lo[name][:, c, o:o + P],
                                       a_hi[:, c, :], a_lo[:, c, :], c == 0, c == CH - 1)
                mm.then_inc(proj_done[layer], 1)

            def output_product(step, layer, d, n):
                pe.wait_ge(ot_lo_done[layer], step.count(PAIRS[layer], d, PAIRS[layer]))
                if step.r is None:
                    pe.wait_ge(w_lo_done, 6 if layer else 4)
                if reader := last_reader(step, n):
                    pe.wait_ge(reader[0], reader[1])
                name = f"o{layer}"
                for ic in range(CH):
                    ps, rows = m_ps[BANK[n]][:, ic * DIM:(ic + 1) * DIM], slice(ic * P, (ic + 1) * P)
                    for c in range(PAIRS[layer]):
                        mm = three(ps, ot_hi[layer][:, c, rows], ot_lo[layer][:, c, rows],
                                   w_hi[name][:, c, :], w_lo[name][:, c, :], c == 0, c == PAIRS[layer] - 1)
                mm.then_inc(wo_done[layer], 1)

            def transpose_rows(step, layer, d, n):
                if layer:
                    src = h
                    pe.wait_ge(ln_done[1], step.count(1, d, 1))
                else:
                    src = x_in[step.parity(d)]
                    pe.wait_ge(x_loaded[step.parity(d)], step.dma(d))
                if reader := last_reader(step, n):
                    pe.wait_ge(reader[0], reader[1])
                for c in range(CH):
                    for ic in range(CH):
                        o = c * NODES + ic * P
                        mm = nc.tensor.transpose(m_ps[BANK[n]][:, o:o + P], src[:, ic, c * P:(c + 1) * P], ident[:])
                mm.then_inc(xt_done[layer], 1)

            def task(step, n, user):
                name, layer, which, d = user
                if not step.has(d):
                    return
                if name == "proj":
                    project(step, layer, which, d, n)
                elif name == "wo":
                    output_product(step, layer, d, n)
                else:
                    transpose_rows(step, layer, d, n)

            pe.wait_ge(consts_done, 1)

            def body(step):
                for name, *which in PE_ORDER:
                    if name == "scores":
                        scores(step, *which)
                    elif name == "transpose":
                        transposes(step, *which)
                    elif name == "pv":
                        attend(step, *which, bank_of((name, *which)))
                    else:
                        task(step, bank_of((name, *which)), (name, *which))

            iterations(pe, body)

        @block.scalar
        def _(act):
            def split_weight(n):
                act.wait_ge(w_loaded[n], 16)
                nc.scalar.activation(w_hi[n][:], w_raw[n][:], ACT.Copy).then_inc(w_hi_done, 1)

            def exponentials(step, k, hh):
                layer, d, pair = slot_of(k)
                if not step.has(d):
                    return
                act.wait_ge(max_done[layer], step.head((layer, d, pair), hh))
                for ic in range(CH):
                    e = nc.scalar.activation(probs[k % 2][:, hh, ic, :], probs[k % 2][:, hh, ic, :], ACT.Exp,
                                             bias=negmax[k % 2][:, hh, ic:ic + 1], scale=-1.0,
                                             accum_out=sums[k % 2][:, hh, ic:ic + 1])
                e.then_inc(exp_done[layer], 1)

            def transposed_hi(step, k, hh):
                layer, d, pair = slot_of(k)
                if not step.has(d):
                    return
                act.wait_ge(t_done[layer], step.head((layer, d, pair), hh))
                nc.scalar.activation(pt_hi[k % 2][:, hh, :, :], t_ps[hh][:].rearrange("p (c i) -> p c i", c=CH),
                                     ACT.Copy).then_inc(pt_hi_done[layer], 1)

            def attended_halves(step, k, n):
                layer, d, pair = slot_of(k)
                if not step.has(d):
                    return
                act.wait_ge(pv_done[layer], step.count(PAIRS[layer], d, pair + 1))
                for hh in range(2):
                    rows, other = slice(hh * HEAD, (hh + 1) * HEAD), slice((1 - hh) * HEAD, (2 - hh) * HEAD)
                    a = nc.scalar.activation(half[k % 2][rows, :], m_ps[BANK[n]][other, hh * NODES:(hh + 1) * NODES],
                                             ACT.Copy)
                a.then_inc(half_done[layer], 1)

            def attended_hi(step, k):
                layer, d, pair = slot_of(k)
                if not step.has(d):
                    return
                act.wait_ge(ot_done[layer], step.count(PAIRS[layer], d, pair + 1))
                nc.scalar.activation(ot_hi[layer][:, pair, :], ot[k % 2][:], ACT.Copy).then_inc(ot_hi_done[layer], 1)

            def task(step, n, user):
                name, layer, which, d = user
                if not step.has(d) or name == "wo":
                    return
                bank = m_ps[BANK[n]]
                if name == "proj":
                    act.wait_ge(proj_done[layer], step.count(PROJ[layer], d, which + 1))
                    what, at = (ORDER_L0, ORDER_L1)[layer][which]
                    if what == "v":
                        dst, src = v_place(layer, at, bank, False)
                    else:
                        dst, src = qk_hi[layer][what][:, 2 * at:2 * at + 2, :], bank[:].rearrange("p (c i) -> p c i", c=2)
                    nc.scalar.activation(dst, src, ACT.Copy).then_inc(proj_hi_done[layer], 1)
                elif name == "xt":
                    act.wait_ge(xt_done[0], step.count(1, d, 1))
                    nc.scalar.activation(xt_hi[0][:], bank[:].rearrange("p (c i) -> p c i", c=CH),
                                         ACT.Copy).then_inc(xt_hi_done[0], 1)
                else:
                    if step.r is None:
                        act.wait_ge(vec_loaded, 64)
                    act.wait_ge(xt_done[1], step.count(1, d, 1))
                    if step.has(d - 1):
                        act.wait_ge(xt_lo_done[1], step.count(1, d - 1, 1))
                    for c in range(CH):
                        a = nc.scalar.activation(ht[:, c, :], bank[:, c * NODES:(c + 1) * NODES], ACT.Identity,
                                                 bias=beta_sb[:, c:c + 1], scale=gamma_sb[:, c:c + 1])
                    a.then_inc(ht_done, 1)

            def body(step):
                for name, *which in ACT_ORDER:
                    if name == "exp":
                        exponentials(step, *which)
                    elif name == "pt":
                        transposed_hi(step, *which)
                    elif name == "half":
                        attended_halves(step, *which, bank_of(("pv", *which)))
                    elif name == "ot":
                        attended_hi(step, *which)
                    elif name == "weight":
                        if step.t == which[0]:
                            split_weight(which[1])
                    else:
                        task(step, bank_of((name, *which)), (name, *which))

            iterations(act, body)

        @block.vector
        def _(dve):
            def split_weight(n):
                dve.wait_ge(w_hi_done, W_NAMES.index(n) + 1)
                nc.vector.tensor_tensor(w_lo[n][:], w_raw[n][:], w_hi[n][:].bitcast(f32),
                                        ALU.subtract).then_inc(w_lo_done, 1)

            def maxima(step, k, hh):
                layer, d, pair = slot_of(k)
                if not step.has(d):
                    return
                dve.wait_ge(mask_done[layer], step.count(1, d, 1))
                dve.wait_ge(s_done[layer], step.head((layer, d, pair), hh))
                step.hold(dve, dve_held)
                for ic in range(CH):
                    m = nc.vector.tensor_tensor_reduce(
                        out=probs[k % 2][:, hh, ic, :], in0=s_ps[hh][:, ic * NODES:(ic + 1) * NODES],
                        in1=mask[layer][step.parity(d)][:, ic, :], scale=-SCALE, scalar=LARGEST,
                        op0=ALU.add, op1=ALU.min, accum_out=negmax[k % 2][:, hh, ic:ic + 1])
                m.then_inc(max_done[layer], 1)

            def reciprocal_sums(step, k, hh):
                layer, d, pair = slot_of(k)
                if not step.has(d):
                    return
                dve.wait_ge(exp_done[layer], step.head((layer, d, pair), hh))
                nc.vector.reciprocal(rsums[k % 2][:, hh, :], sums[k % 2][:, hh, :]).then_inc(rsum_done[layer], 1)

            def transposed_lo(step, k, hh):
                layer, d, pair = slot_of(k)
                if not step.has(d):
                    return
                dve.wait_ge(pt_hi_done[layer], step.head((layer, d, pair), hh))
                nc.vector.tensor_tensor(pt_lo[k % 2][:, hh, :, :], t_ps[hh][:].rearrange("p (c i) -> p c i", c=CH),
                                        pt_hi[k % 2][:, hh, :, :].bitcast(f32), ALU.subtract).then_inc(pt_lo_done[layer], 1)

            def attended_sum(step, k, n):
                layer, d, pair = slot_of(k)
                if not step.has(d):
                    return
                if prev := before(step, k, 2):
                    dve.wait_ge(ot_lo_done[prev[0]], step.count(PAIRS[prev[0]], prev[1], prev[2] + 1))
                dve.wait_ge(half_done[layer], step.count(PAIRS[layer], d, pair + 1))
                for hh in range(2):
                    rows = slice(hh * HEAD, (hh + 1) * HEAD)
                    o = nc.vector.tensor_tensor(ot[k % 2][rows, :], m_ps[BANK[n]][rows, hh * NODES:(hh + 1) * NODES],
                                                half[k % 2][rows, :], ALU.add)
                o.then_inc(ot_done[layer], 1)

            def statistics(step, w, d):
                if not step.has(d):
                    return
                if w == 1:
                    dve.wait_ge(ln_done[0], step.count(1, d, 1))
                else:
                    dve.wait_ge(y_done[w // 2], step.count(1, d, 1))
                for ic in range(CH):
                    b = nc.vector.bn_stats(bn[w][:, ic, :], ln_in[w][:, ic, :])
                b.then_inc(bn_done[w], 1)
                dve.wait_ge(bn_done[w], step.count(1, d, 1))
                step.hold(dve, dve_held)
                for ic in range(CH):
                    b = nc.vector.bn_aggr(stats[w][:, ic, :], bn[w][:, ic, :])
                b.then_inc(stats_done[w], 1)

            def normalise(step, w, d):
                if not step.has(d):
                    return
                dst = ln_out[w] if w < 2 else out_sb[step.parity(d)]
                if w == 0:
                    if step.has(d - 1):
                        dve.wait_ge(xb_done[1], step.count(1, d - 1, 1))
                if w == 1:
                    if step.has(d - 1):
                        dve.wait_ge(xt_done[1], step.count(1, d - 1, 1))
                if w == 2:
                    if step.has(d - 2):
                        dve.wait_ge(out_stored[step.parity(d)], step.dma(d - 2))
                dve.wait_ge(rstd_done[w], step.count(1, d, 1))
                for ic in range(CH):
                    o = nc.vector.tensor_scalar(dst[:, ic, :], ln_in[w][:, ic, :], stats[w][:, ic, 0:1],
                                                rstd[w][:, ic:ic + 1], ALU.subtract, ALU.mult)
                o.then_inc(ln_done[w], 1)

            def task(step, n, user):
                name, layer, which, d = user
                if not step.has(d):
                    return
                bank = m_ps[BANK[n]]
                if name == "proj":
                    dve.wait_ge(proj_hi_done[layer], step.count(PROJ[layer], d, which + 1))
                    what, at = (ORDER_L0, ORDER_L1)[layer][which]
                    if what == "v":
                        (dst, src), (hi, _) = v_place(layer, at, bank, True), v_place(layer, at, bank, False)
                    else:
                        dst, src = qk_lo[layer][what][:, 2 * at:2 * at + 2, :], bank[:].rearrange("p (c i) -> p c i", c=2)
                        hi = qk_hi[layer][what][:, 2 * at:2 * at + 2, :]
                    nc.vector.tensor_tensor(dst, src, hi.bitcast(f32), ALU.subtract).then_inc(proj_lo_done[layer], 1)
                elif name == "xt":
                    dve.wait_ge(xt_hi_done[0], step.count(1, d, 1))
                    nc.vector.tensor_tensor(xt_lo[0][:], bank[:].rearrange("p (c i) -> p c i", c=CH),
                                            xt_hi[0][:].bitcast(f32), ALU.subtract).then_inc(xt_lo_done[0], 1)
                elif name == "ht":
                    dve.wait_ge(ht_done, step.count(1, d, 1))
                    nc.vector.tensor_copy(xt_hi[1][:], ht[:]).then_inc(xt_hi_done[1], 1)
                else:
                    res = x1_b[step.parity(d)] if layer else x_in[step.parity(d)]
                    dve.wait_ge(xb_done[layer], step.count(1, d, 1))
                    dve.wait_ge(wo_done[layer], step.count(1, d, 1))
                    nc.vector.tensor_tensor(y[layer][:], bank[:].rearrange("p (c i) -> p c i", c=CH), res[:],
                                            ALU.add).then_inc(y_done[layer], 1)

            def body(step):
                for name, *which in DVE_ORDER:
                    if name == "max":
                        maxima(step, *which)
                    elif name == "rsum":
                        reciprocal_sums(step, *which)
                    elif name == "pt":
                        transposed_lo(step, *which)
                    elif name == "sum":
                        attended_sum(step, *which, bank_of(("pv", *which)))
                    elif name == "norm":
                        normalise(step, *which)
                    elif name == "stats":
                        statistics(step, *which)
                    elif name == "weight":
                        if step.t == which[0]:
                            split_weight(which[1])
                    else:
                        task(step, bank_of((name, *which)), (name, *which))

            iterations(dve, body)

        @block.gpsimd
        def _(pool):
            nc.gpsimd.memset(minus_half[:], -0.5)
            nc.gpsimd.memset(ident[:], 0.0).then_inc(ident_zeroed, 1)
            pool.wait_ge(ident_zeroed, 1)
            nc.gpsimd.affine_select(out=ident[:], in_=ident[:], compare_op=ALU.not_equal, fill=1.0, base=0,
                                    pattern=[[-1, P]], channel_multiplier=1).then_inc(consts_done, 1)
            pool.wait_ge(consts_done, 1)

            def probabilities(step, k, hh):
                layer, d, pair = slot_of(k)
                if not step.has(d):
                    return
                pool.wait_ge(rsum_done[layer], step.head((layer, d, pair), hh))
                step.hold(pool, pool_held)
                for ic in range(CH):
                    e = probs[k % 2][:, hh, ic, :]
                    o = nc.gpsimd.tensor_scalar(e, e, rsums[k % 2][:, hh, ic:ic + 1], 1.0, ALU.mult, ALU.mult)
                o.then_inc(probs_done[layer], 1)

            def reciprocal_std(step, w, d):
                if not step.has(d):
                    return
                pool.wait_ge(stats_done[w], step.count(1, d, 1))
                step.hold(pool, pool_held)
                nc.gpsimd.tensor_scalar(var_eps[w][:], stats[w][:, :, 1], EPS, 1.0, ALU.add,
                                        ALU.mult).then_inc(var_done[w], 1)
                pool.wait_ge(var_done[w], step.count(1, d, 1))
                nc.gpsimd.tensor_tensor(rstd[w][:], var_eps[w][:], minus_half[:], ALU.pow).then_inc(rstd_done[w], 1)

            def make_mask(step, layer, d):
                if not step.has(d):
                    return
                m = mask[layer][step.parity(d)]
                pool.wait_ge(adj_loaded[step.parity(d)], step.dma(d))
                if step.has(d - 2):
                    pool.wait_ge(max_done[layer], step.count(HEADS[layer], d - 2, HEADS[layer]))
                step.hold(pool, pool_held)
                o = nc.gpsimd.tensor_scalar(m[:], adj_in[step.parity(d)][:], -1.0, (MASKED0, MASKED1)[layer],
                                            ALU.add, ALU.mult)
                if layer == 0:
                    o.then_inc(mask_done[0], 1)
                    return
                o.then_inc(mask_sel, 1)
                pool.wait_ge(mask_sel, step.count(1, d, 1))
                step.hold(pool, pool_held)
                nc.gpsimd.affine_select(out=m[:], in_=m[:], compare_op=ALU.not_equal, fill=0.0, base=0,
                                        pattern=[[P, CH], [-1, NODES]], channel_multiplier=1).then_inc(mask_done[1], 1)

            def add_bias(step, layer, d):
                if not step.has(d):
                    return
                if layer:
                    src, dst = x1, x1_b[step.parity(d)]
                    pool.wait_ge(ln_done[0], step.count(1, d, 1))
                    if step.has(d - 2):
                        pool.wait_ge(y_done[1], step.count(1, d - 2, 1))
                else:
                    src = dst = x_in[step.parity(d)]
                    if step.r is None:
                        pool.wait_ge(vec_loaded, 64)
                    pool.wait_ge(xt_done[0], step.count(1, d, 1))
                for ic in range(CH):
                    o = nc.gpsimd.tensor_tensor(dst[:, ic, :], src[:, ic, :], bias_sb[layer][:], ALU.add)
                o.then_inc(xb_done[layer], 1)

            def ht_lo(step, d):
                if not step.has(d):
                    return
                pool.wait_ge(xt_hi_done[1], step.count(1, d, 1))
                nc.gpsimd.tensor_tensor(xt_lo[1][:], ht[:], xt_hi[1][:].bitcast(f32),
                                        ALU.subtract).then_inc(xt_lo_done[1], 1)

            def attended_lo(step, k):
                layer, d, pair = slot_of(k)
                if not step.has(d):
                    return
                pool.wait_ge(ot_hi_done[layer], step.count(PAIRS[layer], d, pair + 1))
                nc.gpsimd.tensor_tensor(ot_lo[layer][:, pair, :], ot[k % 2][:], ot_hi[layer][:, pair, :].bitcast(f32),
                                        ALU.subtract).then_inc(ot_lo_done[layer], 1)

            def body(step):
                for name, *which in POOL_ORDER:
                    if name == "probs":
                        probabilities(step, *which)
                    elif name == "ot":
                        attended_lo(step, *which)
                    elif name == "rstd":
                        reciprocal_std(step, *which)
                    elif name == "mask":
                        make_mask(step, *which)
                    elif name == "bias":
                        add_bias(step, *which)
                    elif name == "ht":
                        ht_lo(step, *which)

            iterations(pool, body)


_INS = ["x", "adj", "L0_gnn_Wq", "L0_gnn_Wk", "L0_gnn_Wv", "L0_gnn_Wo", "L0_gnn_bo", "L1_gnn_gamma", "L1_gnn_beta",
        "L1_gnn_w_qkv", "L1_gnn_w_out", "L1_gnn_b_out"]
_TRANSPOSED = ("L1_gnn_w_qkv", "L1_gnn_w_out")


def kernel(**inputs):
    import concourse.bacc as _bacc
    from concourse.bass_utils import run_bass_kernel_spmd as _run

    nc = _bacc.Bacc("TRN2", target_bir_lowering=False, num_devices=1)
    arrays, args = {}, []
    for name in _INS:
        a = np.asarray(inputs[name])
        if name in _TRANSPOSED:
            a = a.T
        a = np.ascontiguousarray(a)
        arrays[f"in_{name}"] = a
        args.append(nc.dram_tensor(f"in_{name}", a.shape, mybir.dt.from_np(a.dtype), kind="ExternalInput").ap())
    out = nc.dram_tensor("out_0", (GRAPHS, NODES, DIM), mybir.dt.float32, kind="ExternalOutput").ap()
    build(nc, *args, out)
    r = _run(nc, [arrays], core_ids=[0])
    return r.results[0]["out_0"]
```
